# Optimizing a Trainium2 kernel written in Bass

```python
import numpy as np
import jax
import jax.numpy as jnp

def _softmax(x, axis=-1):
    return jax.nn.softmax(x, axis=axis)

def _gelu(x):
    return jax.nn.gelu(x, approximate=True)

def _silu(x):
    return jax.nn.silu(x)

def _sigmoid(x):
    return jax.nn.sigmoid(x)

def _layernorm(x, axis=-1, eps=1e-05):
    m = jnp.mean(x, axis=axis, keepdims=True)
    v = jnp.var(x, axis=axis, keepdims=True)
    return (x - m) / jnp.sqrt(v + eps)

def _scatter_add(tgt, idx, src, axis=0):
    return tgt.at[idx].add(src)

def _segment_sum(src, seg, n):
    return jax.ops.segment_sum(src, seg, n)
kernel_name = 'mk_adj_preln_d1_adj_r2_474416'

def setup_inputs(seed: int=0):
    np.random.seed(seed)
    _w = jnp.asarray

    def _rec_inputs():
        import jax
        import jax.numpy as jnp
        _gk = jax.random.key(seed)
        x = -9.806e-05 + 1 * jax.random.normal(jax.random.fold_in(_gk, 1), (4096, 64), jnp.float32)
        _a = jax.random.bernoulli(jax.random.fold_in(_gk, 2), 0.00390625, (4096, 4096))
        _af = _a.astype(jnp.float32)
        adj = _af
        return (x, adj)
    x, adj = _rec_inputs()

    def _L0_gnn_setup():
        import jax, jax.numpy as jnp
        import numpy as np
        N, D_IN, D_OUT = (4096, 64, 64)
        MAX_NEIGH = 100
        DECAY = 0.5
        key = jax.random.key(seed)
        k1, k2, k3, k4 = jax.random.split(key, 4)
        stdv = 1.0 / np.sqrt(D_OUT)
        inputs = {'input': jax.random.normal(k1, (N, D_IN), dtype=jnp.float32), 'adj': jax.random.randint(k2, (N, N), 0, 2).astype(jnp.float32), 'weight': jax.random.uniform(k3, (D_IN, D_OUT), minval=-stdv, maxval=stdv, dtype=jnp.float32), 'bias': jax.random.uniform(k4, (D_OUT,), minval=-stdv, maxval=stdv, dtype=jnp.float32)}
        return inputs
    _L0_gnn_all = _L0_gnn_setup()
    _L0_gnn_in = {k: v for k, v in _L0_gnn_all.items() if k in ('weight', 'bias')}
    del _L0_gnn_all
    return {'x': x, 'adj': adj, 'L0_gnn_weight': _L0_gnn_in['weight'], 'L0_gnn_bias': _L0_gnn_in['bias']}

def reference(x, adj, L0_gnn_weight, L0_gnn_bias):
    import jax
    import jax.numpy as jnp

    def _L0_gnn_ref(input, adj, weight, bias):
        import jax, jax.numpy as jnp
        import numpy as np
        N, D_IN, D_OUT = (4096, 64, 64)
        MAX_NEIGH = 100
        DECAY = 0.5
        support = input @ weight
        mask = (adj != 0).astype(support.dtype)
        rank = jnp.cumsum(mask, axis=1)
        deg = rank[:, -1:]
        k = jnp.minimum(deg, float(MAX_NEIGH))
        pos = rank - (deg - k)
        w = mask * jnp.where(pos > 0, DECAY ** (k - pos), 0.0)
        out = w @ support + bias
        return out
    h = jnp.maximum(_layernorm(x, axis=-1), 0.0)
    x = x + _L0_gnn_ref(h, adj, L0_gnn_weight, L0_gnn_bias)
    return x

_drawn_inputs = setup_inputs


def setup_inputs(seed=0):
    import zlib

    import numpy as np

    out = dict(_drawn_inputs(seed))
    spreads = {}
    factors = {}
    for name, (base, spread) in spreads.items():
        noise = np.random.default_rng([zlib.crc32(name.encode()), seed]).standard_normal(out[name].shape)
        drawn = base * np.exp(spread * noise) if base else spread * noise
        out[name] = jnp.asarray(drawn.astype(out[name].dtype))
    for name, factor in factors.items():
        out[name] = (out[name] * factor).astype(out[name].dtype)
    return out
```

```python
import concourse.bass as bass
from concourse import mybir
from contextlib import ExitStack


def gnn_decay_kernel(nc, x, adj, weight, bias, out):
    fp32 = mybir.dt.float32
    bf16 = mybir.dt.bfloat16
    i16 = mybir.dt.int16
    ALU = mybir.AluOpType
    ACT = mybir.ActivationFunctionType
    AX = mybir.AxisListType

    N, D = x.shape
    P = 128
    T = N // P
    NT = N // P
    GT = 4
    NG = NT // GT
    CT = GT // 2
    CW = CT * P
    MAX_NEIGH = 100
    STEP = 128.0
    OWN = MAX_NEIGH * STEP
    SCALE = 2.0 ** (127 - MAX_NEIGH)
    EPS = 1e-5
    LEVELS = T.bit_length() - 1
    RND = 4
    RT = T // RND

    adj_t = adj.rearrange("(n q) j -> n q j", q=P)
    out_g = out.rearrange("(g k q) d -> g q k d", q=P, k=GT)

    ctx = ExitStack()
    with ctx:
        def sb(name, shape, dt):
            return ctx.enter_context(nc.sbuf_tensor(name, shape, dt))

        def pb(name, shape, dt):
            return ctx.enter_context(nc.psum_tensor(name, shape, dt))

        def sem(name):
            return ctx.enter_context(nc.semaphore(name))

        adj_f = sb("adj_f", [P, GT, N], fp32)
        masks = sb("masks", [P, 2, GT, N], bf16)
        part_sums = [sb(f"part_sums{l}", [P, P, T >> (l + 1)], bf16) for l in range(LEVELS - 1)]
        totals = sb("totals", [P, 2, GT, P], bf16)
        totals_t = sb("totals_t", [P, 2, GT * P], bf16)
        w_t = sb("w_t", [P, 2, 2, CW], bf16)
        support = sb("support", [P, T, 3, D], bf16)
        x_rows = sb("x_rows", [P, NT, D], fp32)
        xb = x_rows
        bias_b = sb("bias_b", [P, D], fp32)
        sum_a = sb("sum_a", [P, 2, CT, D], fp32)
        sum_b = sb("sum_b", [P, 2, CT, D], fp32)
        x_cols = sb("x_cols", [P, T, D], fp32)
        cen = sb("cen", [P, T, D], fp32)
        h = x_cols
        h_t = sb("h_t", [P, T // 2, P], fp32)
        rest = sb("rest", [P, T, D], fp32)
        sq = rest
        row_sum = sb("row_sum", [P, T], fp32)
        sq_sum = sb("sq_sum", [P, T], fp32)
        var_eps = sb("var_eps", [P, T], fp32)
        std, rough, newton_a, newton_b = (sb(n, [P, T], fp32) for n in ("std", "rough", "newton_a", "newton_b"))
        rstd = sb("rstd", [P, T], fp32)
        w2 = sb("w2", [P, P], fp32)
        ident_f = sb("ident_f", [P, P], fp32)
        ident = sb("ident", [P, P], bf16)
        diag_own = sb("diag_own", [P, P], bf16)
        diag_past = sb("diag_past", [P, P], bf16)
        behind = sb("behind", [P, P], bf16)

        chain = [pb(f"chain{c}", [P, 512], fp32) for c in range(2)]
        acc = pb("acc", [P, 4, 512], fp32)
        aux = pb("aux", [P, 2, 512], fp32)
        totals_ps = aux[:, 0, 0:GT * P // 2].bitcast(bf16)

        x_loaded = sem("x_loaded")
        rows_loaded = sem("rows_loaded")
        weight_loaded = sem("weight_loaded")
        adj_loaded = [sem(f"adj_loaded{k}") for k in range(GT)]
        zeroed = sem("zeroed")
        w2_zeroed = sem("w2_zeroed")
        consts_ready = sem("consts_ready")
        xb_ready = sem("xb_ready")
        ln_step = sem("ln_step")
        std_ready = sem("std_ready")
        h_ready = sem("h_ready")
        h_turned = sem("h_turned")
        h_t_ready = sem("h_t_ready")
        support_ps_ready = sem("support_ps_ready")
        high_ready = sem("high_ready")
        rest_ready = sem("rest_ready")
        middle_ready = sem("middle_ready")
        mask_ready = sem("mask_ready")
        halved = sem("halved")
        totals_ready = sem("totals_ready")
        totals_turned = sem("totals_turned")
        totals_t_ready = sem("totals_t_ready")
        chain_ready = [sem(f"chain_ready{c}") for c in range(2)]
        w_ready = [sem(f"w_ready{c}") for c in range(2)]
        w_used = [sem(f"w_used{c}") for c in range(2)]
        low_added = sem("low_added")
        middle_added = sem("middle_added")
        acc_freed = sem("acc_freed")
        stored = sem("stored")

        block = ctx.enter_context(nc.Block())

        @block.sync
        def _(sp):
            sp.dma_start(x_cols[:, :, :], x.rearrange("(p t) d -> p t d", t=T)).then_inc(x_loaded, 16)
            for k in range(GT):
                sp.dma_start(adj_f[:, k, :], adj_t[k]).then_inc(adj_loaded[k], 16)
            with sp.Fori(1, NG) as g:
                for k in range(GT):
                    sp.wait_ge(mask_ready, GT * g + (k + 1 - GT))
                    sp.dma_start(adj_f[:, k, :], adj_t[GT * g + k]).then_inc(adj_loaded[k], 16)

        @block.gpsimd
        def _(pool):
            nc.gpsimd.memset(w2[:, :], 0.0).then_inc(w2_zeroed, 1)
            nc.gpsimd.memset(ident_f[:, :], 0.0).then_inc(zeroed, 1)
            nc.gpsimd.memset(ident[:, :], 0.0).then_inc(zeroed, 1)
            nc.gpsimd.memset(diag_own[:, :], 0.0).then_inc(zeroed, 1)
            nc.gpsimd.memset(diag_past[:, :], 0.0).then_inc(zeroed, 1)
            nc.gpsimd.memset(behind[:, :], -STEP).then_inc(zeroed, 1)
            pool.wait_ge(zeroed, 5)
            for m, value in ((ident_f, 1.0), (ident, 1.0), (diag_own, OWN), (diag_past, -(OWN + STEP))):
                nc.gpsimd.affine_select(out=m[:, :], in_=m[:, :], compare_op=ALU.not_equal, fill=value, base=0,
                                        pattern=[[-1, P]], channel_multiplier=1).then_inc(consts_ready, 1)
            nc.gpsimd.affine_select(out=behind[:, :], in_=behind[:, :], compare_op=ALU.is_gt, fill=0.0, base=0,
                                    pattern=[[-1, P]], channel_multiplier=1).then_inc(consts_ready, 1)
            for r in range(RND):
                ts = slice(r * RT, (r + 1) * RT)
                pool.wait_ge(middle_ready, r + 1)
                last = nc.gpsimd.tensor_tensor(support[:, ts, 2, :], rest[:, ts, :], support[:, ts, 1, :],
                                               ALU.subtract)
            last.then_inc(acc_freed, 1)
            pool.wait_ge(rows_loaded, 32)
            nc.gpsimd.tensor_tensor(xb[:, :, :], x_rows[:, :, :],
                                    bias_b[:, :].unsqueeze(1).to_broadcast([P, NT, D]),
                                    ALU.add).then_inc(xb_ready, 1)
            with pool.Fori(0, NG) as g:
                pool.wait_ge(acc_freed, g + 2)
                pool.dma_start(out_g[g], xb[:, bass.ds(GT * g, GT), :]).then_inc(stored, 16)
            pool.wait_ge(stored, 16 * NG)

        @block.scalar
        def _(act):
            act.wait_ge(w2_zeroed, 1)
            act.dma_start(w2[0:D, 0:D], weight).then_inc(weight_loaded, 16)
            act.dma_start(w2[D:2 * D, D:2 * D], weight).then_inc(weight_loaded, 16)
            act.dma_start(x_rows[:, :, :], x.rearrange("(n q) d -> q n d", q=P)).then_inc(rows_loaded, 16)
            act.dma_start(bias_b[:, :], bias.rearrange("(a d) -> a d", a=1).to_broadcast([P, D]))\
               .then_inc(rows_loaded, 16)
            act.wait_ge(ln_step, 5)
            nc.scalar.activation(std[:, :], var_eps[:, :], ACT.Sqrt).then_inc(std_ready, 1)
            for r in range(RND):
                act.wait_ge(h_turned, r + 1)
                nc.scalar.activation(h_t[:, 4 * r:4 * r + 4, :],
                                     aux[:, r % 2, :].rearrange("p (a b) -> p a b", a=4),
                                     ACT.Copy).then_inc(h_t_ready, 1)
            for r in range(RND):
                ts = slice(r * RT, (r + 1) * RT)
                act.wait_ge(support_ps_ready, r + 1)
                nc.scalar.activation(support[:, ts, 0, :], acc[:, r, :].rearrange("p (t d) -> p t d", d=D),
                                     ACT.Copy, scale=SCALE).then_inc(high_ready, 1)
            for r in range(RND):
                ts = slice(r * RT, (r + 1) * RT)
                act.wait_ge(rest_ready, r + 1)
                nc.scalar.activation(support[:, ts, 1, :], rest[:, ts, :], ACT.Copy).then_inc(middle_ready, 1)

            def weigh(c, slot, n, reuse):
                act.wait_ge(chain_ready[c], n + 1)
                if reuse:
                    act.wait_ge(w_used[c], n - 1)
                nc.scalar.activation(w_t[:, c, slot, :].bitcast(i16), chain[c][:, 0:CW],
                                     ACT.Relu).then_inc(w_ready[c], 1)

            for slot in range(2):
                for c in range(2):
                    weigh(c, slot, slot, False)
            with act.Fori(2, NG * T, 2) as n:
                for slot in range(2):
                    for c in range(2):
                        weigh(c, slot, n + slot, True)

        @block.vector
        def _(dve):
            dve.wait_ge(x_loaded, 16)
            nc.vector.reduce_sum(row_sum[:, :], x_cols[:, :, :], AX.X).then_inc(ln_step, 1)
            dve.wait_ge(ln_step, 1)
            nc.vector.scalar_tensor_tensor(out=cen[:, :, :], in0=row_sum[:, :].unsqueeze(2).to_broadcast([P, T, D]),
                                           scalar=-1.0 / D, in1=x_cols[:, :, :], op0=ALU.mult,
                                           op1=ALU.add).then_inc(ln_step, 1)
            dve.wait_ge(ln_step, 2)
            nc.vector.tensor_tensor(sq[:, :, :], cen[:, :, :], cen[:, :, :], ALU.mult).then_inc(ln_step, 1)
            dve.wait_ge(ln_step, 3)
            nc.vector.reduce_sum(sq_sum[:, :], sq[:, :, :], AX.X).then_inc(ln_step, 1)
            dve.wait_ge(ln_step, 4)
            nc.vector.tensor_scalar(var_eps[:, :], sq_sum[:, :], 1.0 / D, EPS, ALU.mult, ALU.add)\
                .then_inc(ln_step, 1)
            dve.wait_ge(std_ready, 1)
            nc.vector.reciprocal(rough[:, :], std[:, :]).then_inc(ln_step, 1)
            dve.wait_ge(ln_step, 6)
            nc.vector.tensor_tensor(newton_a[:, :], rough[:, :], rough[:, :], ALU.mult).then_inc(ln_step, 1)
            dve.wait_ge(ln_step, 7)
            nc.vector.tensor_tensor(newton_b[:, :], newton_a[:, :], var_eps[:, :], ALU.mult).then_inc(ln_step, 1)
            dve.wait_ge(ln_step, 8)
            nc.vector.tensor_scalar(newton_a[:, :], newton_b[:, :], -0.5, 1.5, ALU.mult, ALU.add)\
                .then_inc(ln_step, 1)
            dve.wait_ge(ln_step, 9)
            nc.vector.tensor_tensor(rstd[:, :], newton_a[:, :], rough[:, :], ALU.mult).then_inc(ln_step, 1)
            dve.wait_ge(ln_step, 10)
            nc.vector.scalar_tensor_tensor(out=h[:, :, :], in0=cen[:, :, :], scalar=0.0,
                                           in1=rstd[:, :].unsqueeze(2).to_broadcast([P, T, D]), op0=ALU.max,
                                           op1=ALU.mult).then_inc(h_ready, 1)

            def mask_tile(g, b, k):
                n = GT * g + k
                m = masks[:, b, k, :]
                dve.wait_ge(adj_loaded[k], 16 * g + 16)
                nc.vector.tensor_scalar(m, adj_f[:, k, :], 0.0, None, ALU.not_equal).then_inc(mask_ready, 1)
                dve.wait_ge(mask_ready, n + 1)
                src = m.rearrange("q (p t) -> q p t", t=T)
                for l in range(LEVELS):
                    half = T >> (l + 1)
                    if l:
                        dve.wait_ge(halved, (LEVELS - 1) * n + l)
                    if half > 1:
                        nc.vector.tensor_tensor(part_sums[l][:, :, :], src[:, :, 0:half], src[:, :, half:2 * half],
                                                ALU.add).then_inc(halved, 1)
                        src = part_sums[l]
                    else:
                        nc.vector.tensor_tensor(totals[:, b, k, :], src[:, :, 0], src[:, :, 1],
                                                ALU.add).then_inc(totals_ready, 1)

            def turn_out(g, b):
                dve.wait_ge(totals_turned, g + 1)
                nc.vector.tensor_copy(totals_t[:, b, :], totals_ps).then_inc(totals_t_ready, 1)

            def combine(g, b):
                for c in range(2):
                    dve.wait_ge(w_used[c], T * g + T)
                part = acc[:, 2 * b:2 * b + 2, 0:CT * 3 * D].rearrange("q c (k s d) -> q c k s d", k=CT, s=3)
                rows = xb[:, bass.ds(GT * g, GT), :].rearrange("q (c k) d -> q c k d", c=2)
                nc.vector.tensor_tensor(sum_a[:, :, :, :], part[:, :, :, 2, :], rows, ALU.add).then_inc(low_added, 1)
                dve.wait_ge(low_added, g + 1)
                nc.vector.tensor_tensor(sum_b[:, :, :, :], part[:, :, :, 1, :], sum_a[:, :, :, :],
                                        ALU.add).then_inc(middle_added, 1)
                dve.wait_ge(middle_added, g + 1)
                nc.vector.tensor_tensor(rows, part[:, :, :, 0, :], sum_b[:, :, :, :], ALU.add).then_inc(acc_freed, 1)

            for k in range(GT):
                mask_tile(0, 0, k)
                if k == 1:
                    for r in range(RND):
                        ts = slice(r * RT, (r + 1) * RT)
                        dve.wait_ge(high_ready, r + 1)
                        nc.vector.scalar_tensor_tensor(
                            out=rest[:, ts, :], in0=acc[:, r, :].rearrange("p (t d) -> p t d", d=D), scalar=SCALE,
                            in1=support[:, ts, 0, :], op0=ALU.mult, op1=ALU.subtract).then_inc(rest_ready, 1)
            turn_out(0, 0)
            for k in range(GT):
                mask_tile(1, 1, k)
            turn_out(1, 1)
            dve.wait_ge(xb_ready, 1)
            combine(0, 0)
            with dve.Fori(1, NG // 2) as u:
                for b in range(2):
                    g2 = 2 * u
                    dve.wait_ge(chain_ready[1], T * g2 + T * (b - 1))
                    for k in range(GT):
                        mask_tile(g2 + b, b, k)
                    turn_out(g2 + b, b)
                    combine(g2 + (b - 1), 1 - b)
            combine(NG - 1, 1)

        @block.tensor
        def _(pe):
            pe.wait_ge(consts_ready, 5)
            pe.wait_ge(h_ready, 1)
            for r in range(RND):
                if r >= 2:
                    pe.wait_ge(h_t_ready, r - 1)
                for q in range(4):
                    t = r * RT + 2 * q
                    last = nc.tensor.transpose(aux[:, r % 2, q * P:(q + 1) * P],
                                               h[:, t:t + 2, :].rearrange("p t d -> p (t d)"), ident_f[:, :])
                last.then_inc(h_turned, 1)
            pe.wait_ge(weight_loaded, 32)
            for r in range(RND):
                pe.wait_ge(h_t_ready, r + 1)
                for q in range(4):
                    last = nc.tensor.matmul(acc[:, r, q * P:(q + 1) * P], h_t[:, 4 * r + q, :], w2[:, :],
                                            start=True, stop=True)
                last.then_inc(support_ps_ready, 1)


            def turn_totals(u, j):
                pe.wait_ge(totals_ready, 2 * GT * u + GT * (j + 1))
                for k in range(GT):
                    last = nc.tensor.transpose(totals_ps[:, k * P:(k + 1) * P], totals[:, j % 2, k, :], ident[:, :])
                last.then_inc(totals_turned, 1)

            loop_t = []

            def below(v):
                return T - 2 * v if isinstance(v, int) else loop_t[-1]

            def columns(b, c, k, v, s):
                return masks[:, b, CT * c + k, :].rearrange("q (p t) -> q p t", t=T)[:, :, below(v) - (1 + s)]

            def count(u, j, c, v, s):
                first = v == 0 and s == 0 if isinstance(v, int) else False
                if first:
                    pe.wait_ge(totals_t_ready, 2 * u + (j + 1))
                if not (first and isinstance(u, int) and u == 0 and j == 0):
                    pe.wait_ge(w_ready[c], 2 * T * u + 2 * v + (T * j + s))
                if first:
                    nc.tensor.matmul(chain[c][:, 0:CW], behind[:, :], totals_t[:, j % 2, c * CW:(c + 1) * CW],
                                     start=True, stop=False, skip_group_check=True)
                else:
                    for k in range(CT):
                        nc.tensor.matmul(chain[c][:, k * P:(k + 1) * P], columns(j % 2, c, k, v, s - 1),
                                         diag_past[:, :], start=False, stop=False, skip_group_check=True)
                for k in range(CT):
                    last = nc.tensor.matmul(chain[c][:, k * P:(k + 1) * P], columns(j % 2, c, k, v, s),
                                            diag_own[:, :], start=False, stop=True, skip_group_check=True)
                last.then_inc(chain_ready[c], 1)

            def product(b, c, v, s):
                first = v == 0 and s == 0 if isinstance(v, int) else False
                end = v == T // 2 - 1 and s == 1 if isinstance(v, int) else False
                for k in range(CT):
                    last = nc.tensor.matmul(acc[:, 2 * b + c, k * 3 * D:(k + 1) * 3 * D],
                                            w_t[:, c, s % 2, k * P:(k + 1) * P],
                                            support[:, below(v) - (1 + s), :, :].rearrange("p s d -> p (s d)"),
                                            start=(first and k == 0), stop=end, skip_group_check=True)
                last.then_inc(w_used[c], 1)

            def group(u, j, before, after):
                b = j % 2
                for c in range(2):
                    count(u, j, c, 0, 0)
                    if before:
                        product(1 - b, c, T // 2 - 1, 1)
                pe.wait_ge(acc_freed, 2 * u + max(j, 1))
                for c in range(2):
                    count(u, j, c, 0, 1)
                    product(b, c, 0, 0)
                with pe.Fori(1, T // 2 - 1) as v:
                    loop_t.append(v * (-2) + T)
                    for s in range(2):
                        for c in range(2):
                            count(u, j, c, v, s)
                            product(b, c, v, s - 1)
                if after:
                    turn_totals(u, j + 1)
                for s in range(2):
                    for c in range(2):
                        count(u, j, c, T // 2 - 1, s)
                        product(b, c, T // 2 - 2 + s, 1 - s)

            turn_totals(0, 0)
            group(0, 0, False, True)
            with pe.Fori(0, NG // 2 - 1) as u:
                for j in (1, 2):
                    group(u, j, True, True)
            group(0, NG - 1, True, False)
            for c in range(2):
                pe.wait_ge(w_ready[c], NG * T)
                product(1, c, T // 2 - 1, 1)


_INS = ["x", "adj", "L0_gnn_weight", "L0_gnn_bias"]


def kernel(**inputs):
    import numpy as np
    import concourse.bacc as bacc
    from concourse import mybir as mb
    from concourse.bass_utils import run_bass_kernel_spmd

    nc = bacc.Bacc("TRN2", target_bir_lowering=False, num_devices=1)
    arrays, args = {}, []
    for name in _INS:
        a = np.ascontiguousarray(inputs[name])
        arrays[f"in_{name}"] = a
        args.append(nc.dram_tensor(f"in_{name}", a.shape, mb.dt.from_np(a.dtype), kind="ExternalInput").ap())
    shape = inputs["x"].shape
    args.append(nc.dram_tensor("out_0", shape, mb.dt.float32, kind="ExternalOutput").ap())
    gnn_decay_kernel(nc, *args)
    r = run_bass_kernel_spmd(nc, [arrays], core_ids=[0])
    return r.results[0]["out_0"]
```

```python
import concourse.bass as bass
from concourse import mybir
from contextlib import ExitStack


def gnn_decay_kernel(nc, x, adj, weight, bias, out):
    fp32 = mybir.dt.float32
    bf16 = mybir.dt.bfloat16
    i16 = mybir.dt.int16
    ALU = mybir.AluOpType
    ACT = mybir.ActivationFunctionType
    AX = mybir.AxisListType

    N, D = x.shape
    P = 128
    T = N // P
    NT = N // P
    GT = 4
    NG = NT // GT
    NC = 4
    CT = GT // NC
    CW = CT * P
    TURN = 8
    MAX_NEIGH = 100
    STEP = 128.0
    OWN = MAX_NEIGH * STEP
    SCALE = 2.0 ** (127 - MAX_NEIGH)
    EPS = 1e-5
    LEVELS = T.bit_length() - 1
    RND = 4
    RT = T // RND

    adj_t = adj.rearrange("(n q) j -> n q j", q=P)
    out_g = out.rearrange("(g k q) d -> g q k d", q=P, k=GT)

    ctx = ExitStack()
    with ctx:
        def sb(name, shape, dt):
            return ctx.enter_context(nc.sbuf_tensor(name, shape, dt))

        def pb(name, shape, dt):
            return ctx.enter_context(nc.psum_tensor(name, shape, dt))

        def sem(name):
            return ctx.enter_context(nc.semaphore(name))

        adj_f = sb("adj_f", [P, GT, N], fp32)
        masks = sb("masks", [P, 2, GT, N], bf16)
        part_sums = [sb(f"part_sums{l}", [P, P, T >> (l + 1)], bf16) for l in range(LEVELS - 1)]
        totals = sb("totals", [P, 2, GT, P], bf16)
        totals_t = sb("totals_t", [P, 2, GT * P], bf16)
        w_t = sb("w_t", [P, NC, 2, CW], bf16)
        support = sb("support", [P, T, 3, D], bf16)
        x_rows = sb("x_rows", [P, NT, D], fp32)
        xb = x_rows
        bias_b = sb("bias_b", [P, D], fp32)
        sum_a = sb("sum_a", [P, 2, 2, D], fp32)
        sum_b = sb("sum_b", [P, 2, 2, D], fp32)
        x_cols = sb("x_cols", [P, T, D], fp32)
        cen = sb("cen", [P, T, D], fp32)
        h = x_cols
        h_t = sb("h_t", [P, T // 2, P], fp32)
        rest = sb("rest", [P, T, D], fp32)
        sq = rest
        row_sum = sb("row_sum", [P, T], fp32)
        mean = sb("mean", [P, T], fp32)
        sq_sum = sb("sq_sum", [P, T], fp32)
        var_eps = sb("var_eps", [P, T], fp32)
        std, rough, newton_a, newton_b = (sb(n, [P, T], fp32) for n in ("std", "rough", "newton_a", "newton_b"))
        rstd = sb("rstd", [P, T], fp32)
        w2 = sb("w2", [P, P], fp32)
        ident_f = sb("ident_f", [P, P], fp32)
        ident = sb("ident", [P, P], bf16)
        diag_own = sb("diag_own", [P, P], bf16)
        diag_past = sb("diag_past", [P, P], bf16)
        behind = sb("behind", [P, P], bf16)

        chain = [pb(f"chain{c}", [P, 512], fp32) for c in range(NC)]
        acc = pb("acc", [P, 2, 2, 512], fp32)

        def acc_tile(b, k):
            return acc[:, b, k // 2, k % 2 * 3 * D:(k % 2 + 1) * 3 * D]

        def totals_ps(b, k):
            at = 6 * D + k % 2 * P // 2
            return acc[:, b, k // 2, at:at + P // 2].bitcast(bf16)

        x_loaded = sem("x_loaded")
        rows_loaded = sem("rows_loaded")
        weight_loaded = sem("weight_loaded")
        adj_loaded = [sem(f"adj_loaded{k}") for k in range(GT)]
        zeroed = sem("zeroed")
        w2_zeroed = sem("w2_zeroed")
        consts_ready = sem("consts_ready")
        xb_ready = sem("xb_ready")
        ln_step = sem("ln_step")
        sum_ready = sem("sum_ready")
        mean_ready = sem("mean_ready")
        cen_ready = sem("cen_ready")
        sq_ready = sem("sq_ready")
        std_ready = sem("std_ready")
        h_ready = sem("h_ready")
        h_turned = sem("h_turned")
        h_t_ready = sem("h_t_ready")
        support_ps_ready = sem("support_ps_ready")
        high_ready = sem("high_ready")
        rest_ready = sem("rest_ready")
        middle_ready = sem("middle_ready")
        mask_ready = sem("mask_ready")
        halved = sem("halved")
        totals_ready = sem("totals_ready")
        totals_turned = sem("totals_turned")
        totals_t_ready = sem("totals_t_ready")
        chain_ready = [sem(f"chain_ready{c}") for c in range(NC)]
        w_ready = [sem(f"w_ready{c}") for c in range(NC)]
        w_used = [sem(f"w_used{c}") for c in range(NC)]
        low_added = sem("low_added")
        middle_added = sem("middle_added")
        acc_freed = sem("acc_freed")
        stored = sem("stored")

        block = ctx.enter_context(nc.Block())

        @block.sync
        def _(sp):
            sp.dma_start(x_cols[:, :, :], x.rearrange("(p t) d -> p t d", t=T)).then_inc(x_loaded, 16)
            for k in range(GT):
                sp.dma_start(adj_f[:, k, :], adj_t[k]).then_inc(adj_loaded[k], 16)
            with sp.Fori(1, NG) as g:
                for k in range(GT):
                    sp.wait_ge(mask_ready, GT * g + (k + 1 - GT))
                    sp.dma_start(adj_f[:, k, :], adj_t[GT * g + k]).then_inc(adj_loaded[k], 16)

        @block.gpsimd
        def _(pool):
            nc.gpsimd.memset(w2[:, :], 0.0).then_inc(w2_zeroed, 1)
            nc.gpsimd.memset(ident_f[:, :], 0.0).then_inc(zeroed, 1)
            nc.gpsimd.memset(ident[:, :], 0.0).then_inc(zeroed, 1)
            nc.gpsimd.memset(diag_own[:, :], 0.0).then_inc(zeroed, 1)
            nc.gpsimd.memset(diag_past[:, :], 0.0).then_inc(zeroed, 1)
            nc.gpsimd.memset(behind[:, :], -STEP).then_inc(zeroed, 1)
            pool.wait_ge(zeroed, 5)
            for m, value in ((ident_f, 1.0), (ident, 1.0), (diag_own, OWN), (diag_past, -(OWN + STEP))):
                nc.gpsimd.affine_select(out=m[:, :], in_=m[:, :], compare_op=ALU.not_equal, fill=value, base=0,
                                        pattern=[[-1, P]], channel_multiplier=1).then_inc(consts_ready, 1)
            nc.gpsimd.affine_select(out=behind[:, :], in_=behind[:, :], compare_op=ALU.is_gt, fill=0.0, base=0,
                                    pattern=[[-1, P]], channel_multiplier=1).then_inc(consts_ready, 1)
            pool.wait_ge(mean_ready, 1)
            nc.gpsimd.tensor_tensor(cen[:, :, :], x_cols[:, :, :], mean[:, :].unsqueeze(2).to_broadcast([P, T, D]),
                                    ALU.subtract).then_inc(cen_ready, 1)
            pool.wait_ge(ln_step, 7)
            pool.wait_ge(cen_ready, 1)
            for r in range(RND):
                ts = slice(r * RT, (r + 1) * RT)
                nc.gpsimd.tensor_tensor(h[:, ts, :], cen[:, ts, :],
                                        rstd[:, ts].unsqueeze(2).to_broadcast([P, RT, D]),
                                        ALU.mult).then_inc(h_ready, 1)
            for r in range(RND):
                ts = slice(r * RT, (r + 1) * RT)
                pool.wait_ge(middle_ready, r + 1)
                last = nc.gpsimd.tensor_tensor(support[:, ts, 2, :], rest[:, ts, :], support[:, ts, 1, :],
                                               ALU.subtract)
            last.then_inc(acc_freed, 1)
            pool.wait_ge(rows_loaded, 32)
            nc.gpsimd.tensor_tensor(xb[:, :, :], x_rows[:, :, :],
                                    bias_b[:, :].unsqueeze(1).to_broadcast([P, NT, D]),
                                    ALU.add).then_inc(xb_ready, 1)
            with pool.Fori(0, NG) as g:
                pool.wait_ge(acc_freed, g + 2)
                pool.dma_start(out_g[g], xb[:, bass.ds(GT * g, GT), :]).then_inc(stored, 16)
            pool.wait_ge(stored, 16 * NG)

        @block.scalar
        def _(act):
            act.wait_ge(w2_zeroed, 1)
            act.dma_start(w2[0:D, 0:D], weight).then_inc(weight_loaded, 16)
            act.dma_start(w2[D:2 * D, D:2 * D], weight).then_inc(weight_loaded, 16)
            act.dma_start(bias_b[:, :], bias.rearrange("(a d) -> a d", a=1).to_broadcast([P, D]))\
               .then_inc(rows_loaded, 16)
            act.wait_ge(cen_ready, 1)
            nc.scalar.activation(sq[:, :, :], cen[:, :, :], ACT.Square).then_inc(sq_ready, 1)
            act.wait_ge(ln_step, 2)
            nc.scalar.activation(std[:, :], var_eps[:, :], ACT.Sqrt).then_inc(std_ready, 1)
            for r in range(RND):
                act.wait_ge(h_turned, r + 1)
                nc.scalar.activation(h_t[:, 4 * r:4 * r + 4, :],
                                     chain[r % 2][:, :].rearrange("p (a b) -> p a b", a=4),
                                     ACT.Relu).then_inc(h_t_ready, 1)
            act.dma_start(x_rows[:, :, :], x.rearrange("(n q) d -> q n d", q=P)).then_inc(rows_loaded, 16)
            for r in range(RND):
                ts = slice(r * RT, (r + 1) * RT)
                act.wait_ge(support_ps_ready, r + 1)
                nc.scalar.activation(support[:, ts, 0, :], acc[:, r // 2, r % 2, :].rearrange("p (t d) -> p t d", d=D),
                                     ACT.Copy, scale=SCALE).then_inc(high_ready, 1)
            for r in range(RND):
                ts = slice(r * RT, (r + 1) * RT)
                act.wait_ge(rest_ready, r + 1)
                nc.scalar.activation(support[:, ts, 1, :], rest[:, ts, :], ACT.Copy).then_inc(middle_ready, 1)

            def weigh(c, slot, n, reuse):
                act.wait_ge(chain_ready[c], n + 1)
                if reuse:
                    act.wait_ge(w_used[c], n - 1)
                nc.scalar.activation(w_t[:, c, slot, :].bitcast(i16), chain[c][:, 0:CW],
                                     ACT.Relu).then_inc(w_ready[c], 1)

            for n in range(TURN):
                for c in range(NC):
                    weigh(c, n % 2, n, n >= 2)
            with act.Fori(1, NG * T // TURN) as u:
                for n in range(TURN):
                    for c in range(NC):
                        weigh(c, n % 2, TURN * u + n, True)

        @block.vector
        def _(dve):
            dve.wait_ge(x_loaded, 16)
            nc.vector.reduce_sum(row_sum[:, :], x_cols[:, :, :], AX.X).then_inc(sum_ready, 1)
            dve.wait_ge(sum_ready, 1)
            nc.vector.tensor_scalar(mean[:, :], row_sum[:, :], 1.0 / D, None, ALU.mult).then_inc(mean_ready, 1)

            def mask_tile(g, b, k):
                n = GT * g + k
                m = masks[:, b, k, :]
                dve.wait_ge(adj_loaded[k], 16 * g + 16)
                nc.vector.tensor_scalar(m, adj_f[:, k, :], 0.0, None, ALU.not_equal).then_inc(mask_ready, 1)
                dve.wait_ge(mask_ready, n + 1)
                src = m.rearrange("q (p t) -> q p t", t=T)
                for l in range(LEVELS):
                    half = T >> (l + 1)
                    if l:
                        dve.wait_ge(halved, (LEVELS - 1) * n + l)
                    if half > 1:
                        nc.vector.tensor_tensor(part_sums[l][:, :, :], src[:, :, 0:half], src[:, :, half:2 * half],
                                                ALU.add).then_inc(halved, 1)
                        src = part_sums[l]
                    else:
                        nc.vector.tensor_tensor(totals[:, b, k, :], src[:, :, 0], src[:, :, 1],
                                                ALU.add).then_inc(totals_ready, 1)

            def turn_out(g, b):
                dve.wait_ge(totals_turned, g + 1)
                spare = acc[:, b, :, 6 * D:6 * D + P].bitcast(bf16)
                nc.vector.tensor_copy(totals_t[:, b, :].rearrange("p (h i) -> p h i", h=2), spare).then_inc(totals_t_ready, 1)

            def combine(g, b):
                for c in range(NC):
                    dve.wait_ge(w_used[c], T * g + T)
                part = acc[:, b, :, 0:6 * D].rearrange("q c (k s d) -> q c k s d", k=2, s=3)
                rows = xb[:, bass.ds(GT * g, GT), :].rearrange("q (c k) d -> q c k d", c=2)
                nc.vector.tensor_tensor(sum_a[:, :, :, :], part[:, :, :, 2, :], rows, ALU.add).then_inc(low_added, 1)
                dve.wait_ge(low_added, g + 1)
                nc.vector.tensor_tensor(sum_b[:, :, :, :], part[:, :, :, 1, :], sum_a[:, :, :, :],
                                        ALU.add).then_inc(middle_added, 1)
                dve.wait_ge(middle_added, g + 1)
                nc.vector.tensor_tensor(rows, part[:, :, :, 0, :], sum_b[:, :, :, :], ALU.add).then_inc(acc_freed, 1)

            def rstd_rows():
                dve.wait_ge(sq_ready, 1)
                nc.vector.reduce_sum(sq_sum[:, :], sq[:, :, :], AX.X).then_inc(ln_step, 1)
                dve.wait_ge(ln_step, 1)
                nc.vector.tensor_scalar(var_eps[:, :], sq_sum[:, :], 1.0 / D, EPS, ALU.mult, ALU.add)\
                    .then_inc(ln_step, 1)
                dve.wait_ge(std_ready, 1)
                nc.vector.reciprocal(rough[:, :], std[:, :]).then_inc(ln_step, 1)
                dve.wait_ge(ln_step, 3)
                nc.vector.tensor_tensor(newton_a[:, :], rough[:, :], rough[:, :], ALU.mult).then_inc(ln_step, 1)
                dve.wait_ge(ln_step, 4)
                nc.vector.tensor_tensor(newton_b[:, :], newton_a[:, :], var_eps[:, :], ALU.mult).then_inc(ln_step, 1)
                dve.wait_ge(ln_step, 5)
                nc.vector.tensor_scalar(newton_a[:, :], newton_b[:, :], -0.5, 1.5, ALU.mult, ALU.add)\
                    .then_inc(ln_step, 1)
                dve.wait_ge(ln_step, 6)
                nc.vector.tensor_tensor(rstd[:, :], newton_a[:, :], rough[:, :], ALU.mult).then_inc(ln_step, 1)

            for k in range(GT):
                mask_tile(0, 0, k)
                if k == 0:
                    rstd_rows()
                if k == 2:
                    for r in range(RND):
                        ts = slice(r * RT, (r + 1) * RT)
                        dve.wait_ge(high_ready, r + 1)
                        nc.vector.scalar_tensor_tensor(
                            out=rest[:, ts, :], in0=acc[:, r // 2, r % 2, :].rearrange("p (t d) -> p t d", d=D), scalar=SCALE,
                            in1=support[:, ts, 0, :], op0=ALU.mult, op1=ALU.subtract).then_inc(rest_ready, 1)
            turn_out(0, 0)
            for k in range(GT):
                mask_tile(1, 1, k)
            turn_out(1, 1)
            dve.wait_ge(xb_ready, 1)
            combine(0, 0)
            with dve.Fori(1, NG // 2) as u:
                for b in range(2):
                    g2 = 2 * u
                    dve.wait_ge(chain_ready[NC - 1], T * g2 + T * (b - 1))
                    for k in range(GT):
                        mask_tile(g2 + b, b, k)
                    turn_out(g2 + b, b)
                    combine(g2 + (b - 1), 1 - b)
            combine(NG - 1, 1)

        @block.tensor
        def _(pe):
            pe.wait_ge(consts_ready, 5)
            for r in range(RND):
                pe.wait_ge(h_ready, r + 1)
                if r >= 2:
                    pe.wait_ge(h_t_ready, r - 1)
                for q in range(4):
                    t = r * RT + 2 * q
                    last = nc.tensor.transpose(chain[r % 2][:, q * P:(q + 1) * P],
                                               h[:, t:t + 2, :].rearrange("p t d -> p (t d)"), ident_f[:, :])
                last.then_inc(h_turned, 1)
            pe.wait_ge(weight_loaded, 32)
            for r in range(RND):
                pe.wait_ge(h_t_ready, r + 1)
                for q in range(4):
                    last = nc.tensor.matmul(acc[:, r // 2, r % 2, q * P:(q + 1) * P], h_t[:, 4 * r + q, :], w2[:, :],
                                            start=True, stop=True)
                last.then_inc(support_ps_ready, 1)


            def turn_totals(u, j):
                pe.wait_ge(totals_ready, 2 * GT * u + GT * (j + 1))
                if not (isinstance(u, int) and u == 0 and j < 2):
                    pe.wait_ge(acc_freed, 2 * u + j)
                for k in range(GT):
                    last = nc.tensor.transpose(totals_ps(j % 2, k), totals[:, j % 2, k, :], ident[:, :])
                last.then_inc(totals_turned, 1)

            def columns(b, k, s):
                return masks[:, b, k, :].rearrange("q (p t) -> q p t", t=T)[:, :, T - 1 - s]

            def count(u, j, c, s):
                b = j % 2
                if s == 0 and c == 0:
                    pe.wait_ge(totals_t_ready, 2 * u + (j + 1))
                if not (isinstance(u, int) and u == 0 and j == 0 and s == 0):
                    pe.wait_ge(w_ready[c], 2 * T * u + (T * j + s))
                if s == 0:
                    nc.tensor.matmul(chain[c][:, 0:CW], behind[:, :], totals_t[:, b, c * CW:(c + 1) * CW],
                                     start=True, stop=False, skip_group_check=True)
                else:
                    for k in range(CT):
                        nc.tensor.matmul(chain[c][:, k * P:(k + 1) * P], columns(b, CT * c + k, s - 1),
                                         diag_past[:, :], start=False, stop=False, skip_group_check=True)
                for k in range(CT):
                    last = nc.tensor.matmul(chain[c][:, k * P:(k + 1) * P], columns(b, CT * c + k, s),
                                            diag_own[:, :], start=False, stop=True, skip_group_check=True)
                last.then_inc(chain_ready[c], 1)

            def product(b, c, s):
                for k in range(CT):
                    last = nc.tensor.matmul(acc_tile(b, CT * c + k), w_t[:, c, s % 2, k * P:(k + 1) * P],
                                            support[:, T - 1 - s, :, :].rearrange("p s d -> p (s d)"),
                                            start=(s == 0 and (CT * c + k) % 2 == 0), stop=(s == T - 1),
                                            skip_group_check=True)
                last.then_inc(w_used[c], 1)

            def group(u, j, before, after):
                b = j % 2
                for s in range(T):
                    if s == 1:
                        pe.wait_ge(acc_freed, 2 * u + max(j, 1))
                    if s == T - 2 and after:
                        turn_totals(u, j + 1)
                    for c in range(NC):
                        count(u, j, c, s)
                        if s:
                            product(b, c, s - 1)
                        elif before:
                            product(1 - b, c, T - 1)

            pe.wait_ge(acc_freed, 1)
            turn_totals(0, 0)
            group(0, 0, False, True)
            with pe.Fori(0, NG // 2 - 1) as u:
                for j in (1, 2):
                    group(u, j, True, True)
            group(0, NG - 1, True, False)
            for c in range(NC):
                pe.wait_ge(w_ready[c], NG * T)
                product(1, c, T - 1)


_INS = ["x", "adj", "L0_gnn_weight", "L0_gnn_bias"]


def kernel(**inputs):
    import numpy as np
    import concourse.bacc as bacc
    from concourse import mybir as mb
    from concourse.bass_utils import run_bass_kernel_spmd

    nc = bacc.Bacc("TRN2", target_bir_lowering=False, num_devices=1)
    arrays, args = {}, []
    for name in _INS:
        a = np.ascontiguousarray(inputs[name])
        arrays[f"in_{name}"] = a
        args.append(nc.dram_tensor(f"in_{name}", a.shape, mb.dt.from_np(a.dtype), kind="ExternalInput").ap())
    shape = inputs["x"].shape
    args.append(nc.dram_tensor("out_0", shape, mb.dt.float32, kind="ExternalOutput").ap())
    gnn_decay_kernel(nc, *args)
    r = run_bass_kernel_spmd(nc, [arrays], core_ids=[0])
    return r.results[0]["out_0"]
```

```python
import concourse.bass as bass
from concourse import mybir
from contextlib import ExitStack


def gnn_decay_kernel(nc, x, adj, weight, bias, out):
    fp32 = mybir.dt.float32
    bf16 = mybir.dt.bfloat16
    i16 = mybir.dt.int16
    ALU = mybir.AluOpType
    ACT = mybir.ActivationFunctionType
    AX = mybir.AxisListType

    N, D = x.shape
    P = 128
    T = N // P
    NT = N // P
    GT = 4
    NG = NT // GT
    CHAINS = GT
    LAG = T // 2
    AHEAD = 2
    MAX_NEIGH = 100
    STEP = 128.0
    OWN = 128 * STEP
    FUSED = 11
    FUSED_LAST = 16
    SCALE = 2.0 ** (127 - MAX_NEIGH)
    EPS = 1e-5
    SUMS = 2
    LEVELS = (T // SUMS).bit_length() - 1
    RND = 4
    RT = T // RND
    ROUNDS = range(RND - 1, -1, -1)

    adj_t = adj.rearrange("(q n) j -> n q j", n=NT)
    out_p = out.rearrange("(q m k) d -> m q k d", m=NT // 2, k=2)

    ctx = ExitStack()
    with ctx:
        def sb(name, shape, dt):
            return ctx.enter_context(nc.sbuf_tensor(name, shape, dt))

        def pb(name, shape, dt):
            return ctx.enter_context(nc.psum_tensor(name, shape, dt))

        def sem(name):
            return ctx.enter_context(nc.semaphore(name))

        adj_f = sb("adj_f", [P, GT, N], fp32)
        masks = sb("masks", [P, 2, GT, N], bf16)
        part_sums = [sb(f"part_sums{l}", [P, 2 * P, T >> (l + 1)], bf16) for l in range(LEVELS - 1)]
        sums = sb("sums", [P, 2, GT, P, SUMS], bf16)
        totals_t = sb("totals_t", [P, 2, GT, P], bf16)
        scaled = sb("scaled", [P, 2 * P, FUSED_LAST], bf16)
        w_t = sb("w_t", [P, CHAINS, 2, P], bf16)
        support = sb("support", [P, T, 3, D], bf16)
        bias_b = sb("bias_b", [P, D], fp32)
        sum_a = sb("sum_a", [P, 2, D], fp32)
        sum_b = sb("sum_b", [P, 2, D], fp32)
        x_sb = sb("x_sb", [P, T, D], fp32)
        xb = x_sb
        cen = sb("cen", [P, T, D], fp32)
        h = cen
        h_t = sb("h_t", [P, T // 2, P], fp32)
        rest = sb("rest", [P, T, D], fp32)
        sq = rest
        row_sum = sb("row_sum", [P, T], fp32)
        mean = sb("mean", [P, T], fp32)
        sq_sum = sb("sq_sum", [P, T], fp32)
        var_eps = sb("var_eps", [P, T], fp32)
        std, rough, newton_a, newton_b = (sb(n, [P, T], fp32) for n in ("std", "rough", "newton_a", "newton_b"))
        rstd = sb("rstd", [P, T], fp32)
        w2 = sb("w2", [P, P], fp32)
        ident_f = sb("ident_f", [P, P], fp32)
        ident = sb("ident", [P, P], bf16)
        diag_past = sb("diag_past", [P, P], bf16)
        behind = sb("behind", [P, P], bf16)
        ones = sb("ones", [P, P], bf16)
        offset = sb("offset", [P, P], bf16)

        chain = [pb(f"chain{c}", [P, 512], fp32) for c in range(CHAINS)]
        acc = pb("acc", [P, 2, 2, 512], fp32)

        def support_ps(n):
            return (chain[2], chain[3], acc[:, 1, 0, :], acc[:, 1, 1, :])[n]

        x_loaded = sem("x_loaded")
        bias_loaded = sem("bias_loaded")
        weight_loaded = sem("weight_loaded")
        adj_loaded = [sem(f"adj_loaded{k}") for k in range(GT)]
        zeroed = sem("zeroed")
        w2_zeroed = sem("w2_zeroed")
        consts_ready = sem("consts_ready")
        ln_step = sem("ln_step")
        sum_ready = sem("sum_ready")
        mean_ready = sem("mean_ready")
        cen_ready = sem("cen_ready")
        sq_ready = sem("sq_ready")
        std_ready = sem("std_ready")
        h_ready = sem("h_ready")
        h_turned = sem("h_turned")
        h_t_ready = sem("h_t_ready")
        support_ps_ready = sem("support_ps_ready")
        high_ready = sem("high_ready")
        rest_ready = sem("rest_ready")
        low_ready = sem("low_ready")
        middle_ready = sem("middle_ready")
        mask_ready = sem("mask_ready")
        halved = sem("halved")
        scaled_ready = sem("scaled_ready")
        fused = sem("fused")
        sums_ready = sem("sums_ready")
        totals_turned = sem("totals_turned")
        totals_t_ready = sem("totals_t_ready")
        chain_ready = [sem(f"chain_ready{c}") for c in range(CHAINS)]
        w_ready = [sem(f"w_ready{c}") for c in range(CHAINS)]
        pair_ready = sem("pair_ready")
        low_added = sem("low_added")
        middle_added = sem("middle_added")
        xb_ready = sem("xb_ready")
        rows_done = sem("rows_done")
        stored = sem("stored")

        block = ctx.enter_context(nc.Block())

        @block.sync
        def _(sp):
            sp.dma_start(x_sb[:, :, :], x.rearrange("(p t) d -> p t d", t=T)).then_inc(x_loaded, 16)
            for k in range(GT):
                sp.dma_start(adj_f[:, k, :], adj_t[k]).then_inc(adj_loaded[k], 16)
            with sp.Fori(1, NG) as g:
                for k in range(GT):
                    sp.wait_ge(mask_ready, GT * g + (k + 1 - GT))
                    sp.dma_start(adj_f[:, k, :], adj_t[GT * g + k]).then_inc(adj_loaded[k], 16)
            with sp.Fori(0, 2 * NG) as q:
                sp.wait_ge(rows_done, q + 1)
                sp.dma_start(out_p[q], xb[:, bass.ds(2 * q, 2), :]).then_inc(stored, 16)
            sp.wait_ge(stored, 16 * 2 * NG)

        @block.gpsimd
        def _(pool):
            nc.gpsimd.memset(w2[:, :], 0.0).then_inc(w2_zeroed, 1)
            nc.gpsimd.memset(ident_f[:, :], 0.0).then_inc(zeroed, 1)
            nc.gpsimd.memset(ident[:, :], 0.0).then_inc(zeroed, 1)
            nc.gpsimd.memset(diag_past[:, :], 0.0).then_inc(zeroed, 1)
            nc.gpsimd.memset(behind[:, :], -STEP / OWN).then_inc(zeroed, 1)
            nc.gpsimd.memset(ones[:, :], 1.0).then_inc(consts_ready, 1)
            nc.gpsimd.memset(offset[:, :], -(OWN - MAX_NEIGH * STEP) / P).then_inc(consts_ready, 1)
            pool.wait_ge(zeroed, 4)
            for m, value in ((ident_f, 1.0), (ident, 1.0), (diag_past, -(OWN + STEP) / OWN)):
                nc.gpsimd.affine_select(out=m[:, :], in_=m[:, :], compare_op=ALU.not_equal, fill=value, base=0,
                                        pattern=[[-1, P]], channel_multiplier=1).then_inc(consts_ready, 1)
            nc.gpsimd.affine_select(out=behind[:, :], in_=behind[:, :], compare_op=ALU.is_gt, fill=0.0, base=0,
                                    pattern=[[-1, P]], channel_multiplier=1).then_inc(consts_ready, 1)
            pool.wait_ge(mean_ready, 1)
            nc.gpsimd.tensor_tensor(cen[:, :, :], x_sb[:, :, :], mean[:, :].unsqueeze(2).to_broadcast([P, T, D]),
                                    ALU.subtract).then_inc(cen_ready, 1)
            pool.wait_ge(ln_step, 7)
            pool.wait_ge(cen_ready, 1)
            for r in ROUNDS:
                ts = slice(r * RT, (r + 1) * RT)
                nc.gpsimd.tensor_tensor(h[:, ts, :], cen[:, ts, :],
                                        rstd[:, ts].unsqueeze(2).to_broadcast([P, RT, D]),
                                        ALU.mult).then_inc(h_ready, 1)
            for n, r in enumerate(ROUNDS):
                ts = slice(r * RT, (r + 1) * RT)
                if n:
                    pool.wait_ge(rest_ready, n + 1)
                    nc.gpsimd.tensor_copy(support[:, ts, 1, :], rest[:, ts, :]).then_inc(middle_ready, 1)
                pool.wait_ge(middle_ready, n + 1)
                nc.gpsimd.tensor_tensor(support[:, ts, 2, :], rest[:, ts, :], support[:, ts, 1, :],
                                        ALU.subtract).then_inc(low_ready, 1)
            pool.wait_ge(bias_loaded, 16)
            nc.gpsimd.tensor_tensor(xb[:, :, :], x_sb[:, :, :],
                                    bias_b[:, :].unsqueeze(1).to_broadcast([P, NT, D]),
                                    ALU.add).then_inc(xb_ready, 1)

        @block.scalar
        def _(act):
            act.wait_ge(w2_zeroed, 1)
            act.dma_start(w2[0:D, 0:D], weight).then_inc(weight_loaded, 16)
            act.dma_start(w2[D:2 * D, D:2 * D], weight).then_inc(weight_loaded, 16)
            act.dma_start(bias_b[:, :], bias.rearrange("(a d) -> a d", a=1).to_broadcast([P, D]))\
               .then_inc(bias_loaded, 16)
            act.wait_ge(cen_ready, 1)
            nc.scalar.activation(sq[:, :, :], cen[:, :, :], ACT.Square).then_inc(sq_ready, 1)
            act.wait_ge(ln_step, 2)
            nc.scalar.activation(std[:, :], var_eps[:, :], ACT.Sqrt).then_inc(std_ready, 1)

            def turn_h(n):
                r = ROUNDS[n]
                act.wait_ge(h_turned, n + 1)
                nc.scalar.activation(h_t[:, 4 * r:4 * r + 4, :],
                                     acc[:, 1, n % 2, :].rearrange("p (a b) -> p a b", a=4),
                                     ACT.Relu).then_inc(h_t_ready, 1)

            def high_part(n):
                r = ROUNDS[n]
                act.wait_ge(support_ps_ready, n + 1)
                nc.scalar.activation(support[:, r * RT:(r + 1) * RT, 0, :],
                                     support_ps(n).rearrange("p (t d) -> p t d", d=D),
                                     ACT.Copy, scale=SCALE).then_inc(high_ready, 1)

            def middle_part(n):
                ts = slice(ROUNDS[n] * RT, (ROUNDS[n] + 1) * RT)
                act.wait_ge(rest_ready, n + 1)
                nc.scalar.activation(support[:, ts, 1, :], rest[:, ts, :], ACT.Copy).then_inc(middle_ready, 1)

            def turn_out(v, i):
                b, p = i // 2 % 2, i % 2
                act.wait_ge(totals_turned, 4 * v + (i + 1))
                nc.scalar.activation(totals_t[:, b, 2 * p:2 * p + 2, :],
                                     acc[:, b, p, 0:2 * P].rearrange("p (k i) -> p k i", k=2),
                                     ACT.Copy).then_inc(totals_t_ready, 1)

            def weigh(c, n, slot):
                act.wait_ge(chain_ready[c], n + 1)
                nc.scalar.activation(w_t[:, c, slot, :].bitcast(i16), chain[c][:, :P],
                                     ACT.Relu).then_inc(w_ready[c], 1)

            def phase(v, i, first, last):
                for n in range(LAG):
                    if n == LAG - AHEAD + 1 and i + 1 < 2 * NG:
                        turn_out(v, i + 1)
                    for c in range(CHAINS):
                        m = LAG * (i - c // 2) + n
                        if not (first and c >= 2) and not (last and c < 2):
                            weigh(c, 4 * LAG * v + m, m % 2)

            for n in range(RND):
                turn_h(n)
                if n:
                    high_part(n - 1)
            middle_part(0)
            turn_out(0, 0)
            high_part(RND - 1)
            phase(0, 0, True, False)
            for i in (1, 2, 3):
                phase(0, i, False, False)
            with act.Fori(0, NG // 2 - 2) as v:
                for i in (4, 5, 6, 7):
                    phase(v, i, False, False)
            for i in range(2 * NG - 4, 2 * NG + 1):
                phase(0, i, False, i == 2 * NG)

        @block.vector
        def _(dve):
            dve.wait_ge(x_loaded, 16)
            nc.vector.reduce_sum(row_sum[:, :], x_sb[:, :, :], AX.X).then_inc(sum_ready, 1)
            dve.wait_ge(sum_ready, 1)
            nc.vector.tensor_scalar(mean[:, :], row_sum[:, :], 1.0 / D, None, ALU.mult).then_inc(mean_ready, 1)


            def mask(v, i, h2):
                b, k, g = i // 2 % 2, i % 2 * 2 + h2, i // 2
                dve.wait_ge(adj_loaded[k], 32 * v + 16 * (g + 1))
                if g >= 2:
                    dve.wait_ge(chain_ready[k], 2 * T * v + T * (g - 1))
                nc.vector.tensor_scalar(masks[:, b, k, :], adj_f[:, k, :], 0.0, OWN,
                                        ALU.not_equal, ALU.mult).then_inc(mask_ready, 1)

            def tiles(i):
                b, p = i // 2 % 2, i % 2
                return masks[:, b, 2 * p:2 * p + 2, :].rearrange("q k (p t) -> q (k p) t", t=T)

            def halve(v, i, l):
                b, p = i // 2 % 2, i % 2
                half = T >> (l + 1)
                if l:
                    dve.wait_ge(halved, 4 * (LEVELS - 1) * v + ((LEVELS - 1) * i + l))
                    src = part_sums[l - 1]
                else:
                    dve.wait_ge(mask_ready, 8 * v + 2 * (i + 1))
                    src = tiles(i)
                if half == SUMS and i >= 4:
                    dve.wait_ge(rows_done, 4 * v + (i - 3))
                if half > SUMS:
                    nc.vector.tensor_tensor(part_sums[l][:, :, :], src[:, :, 0:half], src[:, :, half:2 * half],
                                            ALU.add).then_inc(halved, 1)
                else:
                    nc.vector.tensor_tensor(sums[:, b, 2 * p:2 * p + 2, :, :].rearrange("q k p s -> q (k p) s"),
                                            src[:, :, 0:half], src[:, :, half:2 * half],
                                            ALU.add).then_inc(sums_ready, 1)

            def scale(v, i, steps):
                if not (isinstance(v, int) and v == 0 and i == 0):
                    dve.wait_ge(fused, 4 * v + i)
                nc.vector.tensor_scalar(scaled[:, :, 0:steps], tiles(i)[:, :, 1:steps + 1], -(OWN + STEP) / OWN, None,
                                        ALU.mult).then_inc(scaled_ready, 1)

            def fuse(v, i, steps):
                m = tiles(i)
                dve.wait_ge(scaled_ready, 4 * v + (i + 1))
                nc.vector.tensor_tensor(m[:, :, 0:steps], m[:, :, 0:steps], scaled[:, :, 0:steps],
                                        ALU.add).then_inc(fused, 1)

            def combine(v, i, part):
                b, p = i // 2 % 2, i % 2
                ps = acc[:, b, p, 0:6 * D].rearrange("q (k s d) -> q k s d", k=2, s=3)
                rows = xb[:, bass.ds(8 * v + 2 * i, 2), :]
                if part == 0:
                    dve.wait_ge(pair_ready, 4 * v + (i + 1))
                    nc.vector.tensor_tensor(sum_a[:, :, :], ps[:, :, 2, :], rows, ALU.add).then_inc(low_added, 1)
                if part == 1:
                    dve.wait_ge(low_added, 4 * v + (i + 1))
                    nc.vector.tensor_tensor(sum_b[:, :, :], ps[:, :, 1, :], sum_a[:, :, :],
                                            ALU.add).then_inc(middle_added, 1)
                if part == 2:
                    dve.wait_ge(middle_added, 4 * v + (i + 1))
                    nc.vector.tensor_tensor(rows, ps[:, :, 0, :], sum_b[:, :, :], ALU.add).then_inc(rows_done, 1)

            def rest_part(n):
                ts = slice(ROUNDS[n] * RT, (ROUNDS[n] + 1) * RT)
                dve.wait_ge(high_ready, n + 1)
                nc.vector.scalar_tensor_tensor(
                    out=rest[:, ts, :], in0=support_ps(n).rearrange("p (t d) -> p t d", d=D), scalar=SCALE,
                    in1=support[:, ts, 0, :], op0=ALU.mult, op1=ALU.subtract).then_inc(rest_ready, 1)

            def rstd_rows():
                dve.wait_ge(sq_ready, 1)
                nc.vector.reduce_sum(sq_sum[:, :], sq[:, :, :], AX.X).then_inc(ln_step, 1)
                dve.wait_ge(ln_step, 1)
                nc.vector.tensor_scalar(var_eps[:, :], sq_sum[:, :], 1.0 / D, EPS, ALU.mult, ALU.add)\
                    .then_inc(ln_step, 1)
                dve.wait_ge(std_ready, 1)
                nc.vector.reciprocal(rough[:, :], std[:, :]).then_inc(ln_step, 1)
                dve.wait_ge(ln_step, 3)
                nc.vector.tensor_tensor(newton_a[:, :], rough[:, :], rough[:, :], ALU.mult).then_inc(ln_step, 1)
                dve.wait_ge(ln_step, 4)
                nc.vector.tensor_tensor(newton_b[:, :], newton_a[:, :], var_eps[:, :], ALU.mult).then_inc(ln_step, 1)
                dve.wait_ge(ln_step, 5)
                nc.vector.tensor_scalar(newton_a[:, :], newton_b[:, :], -0.5, 1.5, ALU.mult, ALU.add)\
                    .then_inc(ln_step, 1)
                dve.wait_ge(ln_step, 6)
                nc.vector.tensor_tensor(rstd[:, :], newton_a[:, :], rough[:, :], ALU.mult).then_inc(ln_step, 1)

            mask(0, 0, 0)
            rstd_rows()
            mask(0, 0, 1)
            for l in range(LEVELS):
                halve(0, 0, l)
                if l == 2:
                    rest_part(0)
            rest_part(1)

            def pair(v, i):
                mask(v, i, 0)
                if i == 1:
                    rest_part(2)
                mask(v, i, 1)
                for l in range(LEVELS):
                    halve(v, i, l)
                    if i == 1 and l == 0:
                        rest_part(3)
                    if i >= 4 and l < 3:
                        combine(v, i - 4, l)
                    if l == 1:
                        scale(v, i - 1, FUSED)
                    if l == 2:
                        fuse(v, i - 1, FUSED)

            for i in (1, 2, 3):
                pair(0, i)
            dve.wait_ge(xb_ready, 1)
            with dve.Fori(0, NG // 2 - 1) as v:
                for i in (4, 5, 6, 7):
                    pair(v, i)
            scale(NG // 2 - 1, 3, FUSED_LAST)
            fuse(NG // 2 - 1, 3, FUSED_LAST)
            for i in range(4):
                for part in range(3):
                    combine(NG // 2 - 1, i, part)

        @block.tensor
        def _(pe):
            pe.wait_ge(consts_ready, 6)

            def turn_h(n):
                pe.wait_ge(h_ready, n + 1)
                if n >= 2:
                    pe.wait_ge(h_t_ready, n - 1)
                for q in range(4):
                    t = ROUNDS[n] * RT + 2 * q
                    last = nc.tensor.transpose(acc[:, 1, n % 2, q * P:(q + 1) * P],
                                               h[:, t:t + 2, :].rearrange("p t d -> p (t d)"), ident_f[:, :])
                last.then_inc(h_turned, 1)

            def make_support(n):
                pe.wait_ge(h_t_ready, n + 1)
                for q in range(4):
                    last = nc.tensor.matmul(support_ps(n)[:, q * P:(q + 1) * P], h_t[:, 4 * ROUNDS[n] + q, :],
                                            w2[:, :], start=True, stop=True)
                last.then_inc(support_ps_ready, 1)

            pe.wait_ge(weight_loaded, 32)
            for n in range(RND):
                turn_h(n)
                if n:
                    make_support(n - 1)


            def turn_totals(u, j, p):
                q = 2 * j + p
                pe.wait_ge(sums_ready, 4 * u + (q + 1))
                for k in (2 * p, 2 * p + 1):
                    at = k % 2 * P
                    for n in range(SUMS):
                        last = nc.tensor.matmul(acc[:, j % 2, p, at:at + P], sums[:, j % 2, k, :, n], ident[:, :],
                                                start=(k % 2 == 0 and n == 0), stop=(n == SUMS - 1),
                                                skip_group_check=True)
                last.then_inc(totals_turned, 1)

            def columns(b, c, s):
                return masks[:, b, c, :].rearrange("q (p t) -> q p t", t=T)[:, :, T - 1 - s]

            def count(u, j, c, s):
                b = j % 2
                steps = FUSED_LAST if j == NG - 1 and c >= 2 else FUSED
                if s == 0:
                    pe.wait_ge(totals_t_ready, 4 * u + (2 * j + c // 2 + 1))
                if not (isinstance(u, int) and u == 0 and j == 0 and s == 0):
                    pe.wait_ge(w_ready[c], 2 * T * u + (T * j + s))
                if s == T - steps:
                    pe.wait_ge(fused, 4 * u + (2 * j + c // 2 + 1))
                if s == 0:
                    nc.tensor.matmul(chain[c][:, :P], behind[:, :], totals_t[:, b, c, :],
                                     start=True, stop=False, skip_group_check=True)
                    nc.tensor.matmul(chain[c][:, :P], offset[:, :], ones[:, :],
                                     start=False, stop=False, skip_group_check=True)
                elif s < T - steps:
                    nc.tensor.matmul(chain[c][:, :P], columns(b, c, s - 1), diag_past[:, :],
                                     start=False, stop=False, skip_group_check=True)
                nc.tensor.matmul(chain[c][:, :P], columns(b, c, s), ident[:, :],
                                 start=False, stop=True, skip_group_check=True).then_inc(chain_ready[c], 1)

            def product(b, c, s):
                at = c % 2 * 3 * D
                mm = nc.tensor.matmul(acc[:, b, c // 2, at:at + 3 * D], w_t[:, c, s % 2, :],
                                      support[:, T - 1 - s, :, :].rearrange("p s d -> p (s d)"),
                                      start=(s == 0 and c % 2 == 0), stop=(s == T - 1), skip_group_check=True)
                if s == T - 1 and c % 2:
                    mm.then_inc(pair_ready, 1)

            def beat(u, j, c, s, first):
                count(u, j, c, s)
                if s:
                    if first and c < 2 and (s - 1) % RT == 0:
                        pe.wait_ge(low_ready, (s - 1) // RT + 1)
                    product(j % 2, c, s - 1)
                elif not first:
                    product(1 - j % 2, c, T - 1)

            def group(u, j, first, after):
                for s in range(T):
                    if s == LAG - AHEAD:
                        turn_totals(u, j, 1)
                    if s == T - AHEAD and after:
                        turn_totals(u, j + 1, 0)
                    for c in (0, 1):
                        beat(u, j, c, s, first)
                    for c in (2, 3):
                        if s >= LAG:
                            beat(u, j, c, s - LAG, first)
                        elif not first:
                            beat(u, j - 1, c, s + T - LAG, False)

            turn_totals(0, 0, 0)
            make_support(RND - 1)
            group(0, 0, True, True)
            with pe.Fori(0, NG // 2 - 1) as u:
                for j in (1, 2):
                    group(u, j, False, True)
            group(0, NG - 1, False, False)
            for c in (0, 1):
                pe.wait_ge(w_ready[c], NG * T)
                product(1, c, T - 1)
            for s in range(T - LAG, T):
                for c in (2, 3):
                    beat(0, NG - 1, c, s, False)
            for c in (2, 3):
                pe.wait_ge(w_ready[c], NG * T)
                product(1, c, T - 1)


_INS = ["x", "adj", "L0_gnn_weight", "L0_gnn_bias"]


def kernel(**inputs):
    import numpy as np
    import concourse.bacc as bacc
    from concourse import mybir as mb
    from concourse.bass_utils import run_bass_kernel_spmd

    nc = bacc.Bacc("TRN2", target_bir_lowering=False, num_devices=1)
    arrays, args = {}, []
    for name in _INS:
        a = np.ascontiguousarray(inputs[name])
        arrays[f"in_{name}"] = a
        args.append(nc.dram_tensor(f"in_{name}", a.shape, mb.dt.from_np(a.dtype), kind="ExternalInput").ap())
    shape = inputs["x"].shape
    args.append(nc.dram_tensor("out_0", shape, mb.dt.float32, kind="ExternalOutput").ap())
    gnn_decay_kernel(nc, *args)
    r = run_bass_kernel_spmd(nc, [arrays], core_ids=[0])
    return r.results[0]["out_0"]
```
